# Optimizing a Trainium2 kernel written in Bass

```python
import numpy as np
import jax
import jax.numpy as jnp

def _softmax(x, axis=-1):
    return jax.nn.softmax(x, axis=axis)

def _gelu(x):
    return jax.nn.gelu(x, approximate=True)

def _silu(x):
    return jax.nn.silu(x)

def _sigmoid(x):
    return jax.nn.sigmoid(x)

def _layernorm(x, axis=-1, eps=1e-05):
    m = jnp.mean(x, axis=axis, keepdims=True)
    v = jnp.var(x, axis=axis, keepdims=True)
    return (x - m) / jnp.sqrt(v + eps)

def _scatter_add(tgt, idx, src, axis=0):
    return tgt.at[idx].add(src)

def _segment_sum(src, seg, n):
    return jax.ops.segment_sum(src, seg, n)
kernel_name = 'mk_seq_postln_d1_jaxref_r8_2f11e6'

def setup_inputs(seed: int=0):
    np.random.seed(seed)
    _w = jnp.asarray

    def _L0_attn_setup():
        import jax, jax.numpy as jnp
        import numpy as np
        EMBED = 128
        WIN = 128
        NUM_HEADS = 16
        HQ = 16
        HKV = 4
        HEAD_DIM = EMBED // NUM_HEADS
        G = HQ // HKV
        key = jax.random.key(seed)
        k = jax.random.split(key, 5)
        B, S = (1, 256)
        x = jax.random.normal(k[0], (B, S, EMBED), dtype=jnp.float32)
        Wq = jax.random.normal(k[1], (HQ * HEAD_DIM, EMBED), dtype=jnp.float32) * 0.02
        Wk = jax.random.normal(k[2], (HKV * HEAD_DIM, EMBED), dtype=jnp.float32) * 0.02
        Wv = jax.random.normal(k[3], (HKV * HEAD_DIM, EMBED), dtype=jnp.float32) * 0.02
        Wo = jax.random.normal(k[4], (EMBED, HQ * HEAD_DIM), dtype=jnp.float32) * 0.02
        return {'x': x, 'Wq': Wq, 'Wk': Wk, 'Wv': Wv, 'Wo': Wo}
    _L0_attn_in = _L0_attn_setup()

    def _L0_ffn_setup():
        import jax, jax.numpy as jnp
        import numpy as np
        TOP_K = 2
        key = jax.random.key(seed)
        ks = jax.random.split(key, 5)
        B, T, D, E, F = (2, 256, 128, 8, 256)
        scale_d = 1.0 / np.sqrt(D)
        scale_f = 1.0 / np.sqrt(F)
        return {'x': jax.random.normal(ks[0], (B, T, D), jnp.float32), 'kernel_router_DE': jax.random.normal(ks[1], (D, E), jnp.float32) * scale_d, 'kernel_gating_EDF': jax.random.normal(ks[2], (E, D, F), jnp.float32) * scale_d, 'kernel_up_EDF': jax.random.normal(ks[3], (E, D, F), jnp.float32) * scale_d, 'kernel_down_EFD': jax.random.normal(ks[4], (E, F, D), jnp.float32) * scale_f}
    _L0_ffn_in = _L0_ffn_setup()
    _d = {'L0_attn_x': _L0_attn_in['x'], 'L0_attn_Wq': _L0_attn_in['Wq'], 'L0_attn_Wk': _L0_attn_in['Wk'], 'L0_attn_Wv': _L0_attn_in['Wv'], 'L0_attn_Wo': _L0_attn_in['Wo'], 'L0_ffn_kernel_router_DE': _L0_ffn_in['kernel_router_DE'], 'L0_ffn_kernel_gating_EDF': _L0_ffn_in['kernel_gating_EDF'], 'L0_ffn_kernel_up_EDF': _L0_ffn_in['kernel_up_EDF'], 'L0_ffn_kernel_down_EFD': _L0_ffn_in['kernel_down_EFD']}
    _x0 = _d['L0_attn_x']
    _d['L0_attn_x'] = jax.random.normal(jax.random.fold_in(jax.random.key(seed), 1), (2, 2048, 128), dtype=_x0.dtype)
    del _x0
    return _d

def reference(L0_attn_x, L0_attn_Wq, L0_attn_Wk, L0_attn_Wv, L0_attn_Wo, L0_ffn_kernel_router_DE, L0_ffn_kernel_gating_EDF, L0_ffn_kernel_up_EDF, L0_ffn_kernel_down_EFD):

    def _L0_attn_ref(x, Wq, Wk, Wv, Wo):
        import jax, jax.numpy as jnp
        import numpy as np
        EMBED = 128
        WIN = 128
        NUM_HEADS = 16
        HQ = 16
        HKV = 4
        HEAD_DIM = EMBED // NUM_HEADS
        G = HQ // HKV
        B, S, _ = x.shape
        W = 2 * WIN + 1
        scale = 1.0 / np.sqrt(HEAD_DIM).astype(np.float32)
        Q = (x @ Wq.T).reshape(B, S, HKV, G, HEAD_DIM)
        K = (x @ Wk.T).reshape(B, S, HKV, HEAD_DIM)
        V = (x @ Wv.T).reshape(B, S, HKV, HEAD_DIM)
        offs = jnp.arange(W) - WIN
        idx = jnp.arange(S)[:, None] + offs[None, :]
        valid = (idx >= 0) & (idx < S)
        idxc = jnp.clip(idx, 0, S - 1)
        K_win = K[:, idxc]
        V_win = V[:, idxc]
        scores = jnp.einsum('bskgd,bswkd->bskgw', Q, K_win) * scale
        scores = jnp.where(valid[None, :, None, None, :], scores, jnp.float32(-jnp.inf))
        attn = jax.nn.softmax(scores, axis=-1)
        out = jnp.einsum('bskgw,bswkd->bskgd', attn, V_win)
        out = out.reshape(B, S, HQ * HEAD_DIM)
        return out @ Wo.T

    def _L0_ffn_ref(x, kernel_router_DE, kernel_gating_EDF, kernel_up_EDF, kernel_down_EFD):
        import jax, jax.numpy as jnp
        import numpy as np
        TOP_K = 2
        E = kernel_router_DE.shape[-1]
        x = x.astype(jnp.float32)
        router_logits_BTE = jnp.einsum('BTD,DE->BTE', x, kernel_router_DE)
        probs_BTE = jax.nn.softmax(router_logits_BTE.astype(jnp.float32), axis=-1)
        weights_BTX, indices_BTX = jax.lax.top_k(probs_BTE, TOP_K)
        norm_weights_BTX = jax.nn.softmax(weights_BTX, axis=-1)
        one_hot_BTXE = jax.nn.one_hot(indices_BTX, num_classes=E, dtype=jnp.float32)
        full_weights_BTE = jnp.sum(one_hot_BTXE * norm_weights_BTX[..., None], axis=2)
        gating_BTEF = jnp.einsum('BTD,EDF->BTEF', x, kernel_gating_EDF)
        fuse_BTEF = jax.nn.silu(gating_BTEF) * jnp.einsum('BTD,EDF->BTEF', x, kernel_up_EDF)
        down_BTED = jnp.einsum('BTEF,EFD->BTED', fuse_BTEF, kernel_down_EFD)
        out_BTD = jnp.einsum('BTED,BTE->BTD', down_BTED, full_weights_BTE)
        return out_BTD.astype(jnp.float32)
    x = L0_attn_x
    x = _layernorm(x + _L0_attn_ref(x, L0_attn_Wq, L0_attn_Wk, L0_attn_Wv, L0_attn_Wo), axis=-1)
    x = _layernorm(x + _L0_ffn_ref(x, L0_ffn_kernel_router_DE, L0_ffn_kernel_gating_EDF, L0_ffn_kernel_up_EDF, L0_ffn_kernel_down_EFD), axis=-1)
    return x

_drawn_inputs = setup_inputs


def setup_inputs(seed=0):
    import zlib

    import numpy as np

    out = dict(_drawn_inputs(seed))
    spreads = {}
    factors = {'L0_attn_Wq': 8.0, 'L0_attn_Wk': 8.0, 'L0_attn_Wv': 2.886}
    for name, (base, spread) in spreads.items():
        noise = np.random.default_rng([zlib.crc32(name.encode()), seed]).standard_normal(out[name].shape)
        drawn = base * np.exp(spread * noise) if base else spread * noise
        out[name] = jnp.asarray(drawn.astype(out[name].dtype))
    for name, factor in factors.items():
        out[name] = (out[name] * factor).astype(out[name].dtype)
    return out
```

```python
from contextlib import ExitStack

import numpy as np

import concourse.bass as bass
from concourse import mybir

F32 = mybir.dt.float32
F32R = mybir.dt.float32r
BF16 = mybir.dt.bfloat16
I32 = mybir.dt.int32
ALU = mybir.AluOpType
ACT = mybir.ActivationFunctionType
AX = mybir.AxisListType

P = 128
D = 128
SEQ = 2048
NB = 2
TOK = NB * SEQ
NT = TOK // P
TPS = SEQ // P
KV, G, HD = 4, 4, 8
C = 32
CH = P // C
VW = 64
QC = P
TC = CH * QC
NU = 9
E, F = 8, 256
FH = F // P
SCALE = 1.0 / float(np.sqrt(np.float32(HD)))
BIG = 1e30
EPS = 1e-5
NG = NT // 4
NH = E * FH
LN_OPS = 15
LN2_OPS = 23
RT_OPS = 23
RSQRT_SEED = 0x5F3759DF

C_ID, C_FLAG, C_REV, C_MASK = 0, P, P + NT, P + NT + E
C_END = C_MASK + 6 * P
ONE_Q, A_LEFT, A_RIGHT, ONE_K, B_LEFT, B_RIGHT, BLOCK = 0, 1, 2, 3, 4, 5, 6

A_UNITS = [(0, 0), (0, 1), (1, 0), (2, 0), (3, 0), (1, 1), (2, 1), (3, 1), None]


def attention_moe(nc, x, xT, wq, wk, wv, wo, wr, wg, wu, wd, consts, kx_rows, blocks, out, v_scr):
    with ExitStack() as ctx:
        def sb(name, shape, dt=F32):
            return ctx.enter_context(nc.sbuf_tensor(name, shape, dt))

        def pb(name):
            return ctx.enter_context(nc.psum_tensor(name, [P, 512], F32))

        def sem(name):
            return ctx.enter_context(nc.semaphore(name))

        cst = sb("cst", [P, C_END])
        blk = sb("blk", [P, KV])
        ident = cst[:, C_ID:C_ID + P]
        mask = sb("mask", [C, 6, P], BF16)
        wq_sb = sb("wq_sb", [P, G, P])
        wk_sb = sb("wk_sb", [P, 96])
        wv_sb = sb("wv_sb", [P, KV * HD])
        wo_sb = sb("wo_sb", [P, D])
        wr_sb = sb("wr_sb", [P, E])
        xt = sb("xt", [P, 4, P])
        z = sb("z", [P, NT, D])
        x1h = sb("x1h", [P, TOK], F32R)
        x1l = sb("x1l", [P, TOK], F32R)
        q = sb("q", [P, 4, TC], F32R)
        kt = sb("kt", [96, P], F32R)
        kx = sb("kx", [P, 4, CH, KV, C], F32R)
        vn = sb("vn", [P, 2, KV * HD])
        vx = sb("vx", [P, 4, CH, VW])
        vx_e = vx[:, :, :, 0:KV * (HD + 1)].rearrange("p s c (v e) -> p s c v e", v=KV)
        probs = sb("probs", [P, 2, NU, TC])
        mp = sb("mp", [P, 3, CH, KV])
        nm = sb("nm", [P, CH, KV])
        oT = sb("oT", [P, 2 * QC])
        rden = sb("rden", [P // 2, G, 2, KV])
        att = sb("att", [P // 2, 2, G, KV, HD])
        attT = sb("attT", [P, P])
        st6 = sb("st6", [P, 4, 6])
        mv = sb("mv", [P, 4, 2])
        nw = sb("nw", [P, 4, 4])
        x1s = sb("x1s", [P, 4, D])
        x1T = sb("x1T", [P, TC])
        rt = sb("rt", [P, 8, 4, E])
        rs = sb("rs", [P, 12, 4])
        wt = sb("wt", [P, NT, E])
        raw = sb("raw", [P, 2, 1024])
        gh = sb("gh", [P, E * F], F32R)
        gl = sb("gl", [P, E * F], F32R)
        uh = sb("uh", [P, E * F], F32R)
        ul = sb("ul", [P, E * F], F32R)
        wd_sb = sb("wd_sb", [P, NH, D])
        sg = probs[:, 0, 0:2, :]
        hid = probs[:, 0, 2:6, :]

        def rt_v(i):
            return rt[:, i]

        pA = [pb("pA0"), pb("pA1")]
        pB = [pb("pB0"), pb("pB1")]
        pW = pb("pW")
        pQ = pb("pQ")
        pM = pb("pM")
        pO = pb("pO")

        s_cst = sem("s_cst")
        s_x0 = sem("s_x0")
        s_z = sem("s_z")
        s_kxr = sem("s_kxr")
        s_zero = sem("s_zero")
        s_ones = sem("s_ones")
        s_const = sem("s_const")
        s_raw = [sem(f"s_raw{i}") for i in range(4)]
        s_wd = sem("s_wd")
        s_split = sem("s_split")
        xt_in = sem("xt_in")
        kv_psum = sem("kv_psum")
        q_psum = sem("q_psum")
        k_hi = sem("k_hi")
        k_lo = sem("k_lo")
        v_copied = sem("v_copied")
        q_hi = sem("q_hi")
        q_lo = sem("q_lo")
        k_spread = sem("k_spread")
        v_out = sem("v_out")
        v_in = sem("v_in")
        a_psum = sem("a_psum")
        a_max = sem("a_max")
        nm_done = sem("nm_done")
        m_psum = sem("m_psum")
        m_in_q = sem("m_in_q")
        b_psum = sem("b_psum")
        exp_done = sem("exp_done")
        pv_done = sem("pv_done")
        oT_done = sem("oT_done")
        o_psum = sem("o_psum")
        den_done = sem("den_done")
        att_done = sem("att_done")
        attT_psum = sem("attT_psum")
        attT_done = sem("attT_done")
        y_psum = sem("y_psum")
        z_done = sem("z_done")
        st_done = sem("st_done")
        mv_done = sem("mv_done")
        ln_ops = sem("ln_ops")
        x1_kept = sem("x1_kept")
        x1T_psum = sem("x1T_psum")
        x1T_done = sem("x1T_done")
        x1h_done = sem("x1h_done")
        x1l_done = sem("x1l_done")
        lg_psum = sem("lg_psum")
        rt_ops = sem("rt_ops")
        rt_exp = sem("rt_exp")
        g_psum = sem("g_psum")
        u_psum = sem("u_psum")
        sg_done = sem("sg_done")
        h_done = sem("h_done")
        d_psum = sem("d_psum")
        acc_done = sem("acc_done")
        ln2_ops = sem("ln2_ops")
        s_out = sem("s_out")

        def has(t):
            return not isinstance(t, int) or 0 <= t < NT

        def wait(eng, s, n):
            if not isinstance(n, int) or n > 0:
                eng.wait_ge(s, n)

        def upto(n):
            return min(n, NT) if isinstance(n, int) else n

        FIRST, LOOP0, LOOPS, LAST = -2, 6, 5, NT + 6

        def steps(eng, step):
            def group(s, c):
                n = (s - c) // 4
                return n if (s - c) % 4 == 0 and 0 <= n < NG else None

            for s in range(FIRST, LOOP0):
                step(s, s % 4, group(s, 7), group(s, 8), group(s, 9))
            with eng.Fori(1, 1 + LOOPS) as it:
                for c in range(2, 6):
                    step(it * 4 + c, c % 4, it - 1 if c == 3 else None, it - 1 if c == 4 else None,
                         it - 1 if c == 5 else None)
            for s in range(LOOP0 + 4 * LOOPS, LAST):
                step(s, s % 4, group(s, 7), group(s, 8), group(s, 9))

        block = ctx.enter_context(nc.Block())

        @block.sync
        def _(sp):
            sp.dma_start(xt[:].rearrange("p s t -> p (s t)"), xT[:, 0:4 * P]).then_inc(s_x0, 16)
            for dst, src in ((wk_sb, wk), (wv_sb, wv), (wq_sb, wq), (blk, blocks), (cst, consts), (wo_sb, wo),
                             (wr_sb, wr)):
                sp.dma_start(dst[:], src).then_inc(s_cst, 16)
            sp.dma_start(probs[96:P, 1, 0:4, :], kx_rows).then_inc(s_kxr, 16)
            sp.dma_start(z[:], x.rearrange("(t p) d -> p t d", p=P)).then_inc(s_z, 16)
            sp.dma_start(raw[:, 0, :], wg[:, 0:1024]).then_inc(s_raw[0], 16)
            sp.dma_start(raw[:, 1, :], wg[:, 1024:2048]).then_inc(s_raw[1], 16)
            sp.dma_start(wd_sb[:], wd).then_inc(s_wd, 16)
            sp.wait_ge(s_zero, 2)

            x_tiles = xT.rearrange("d (n t) -> d n t", t=P)

            def value(n):
                return n if isinstance(n, int) else sp.snap(sp.to_reg(n))

            def step(s, j, ln, tr, rt):
                x4, v, k = s + 5, s + 1, s + 2
                x_used, x_before, at_x = value(s + 2), value(16 * (x4 - 4)), value(x4)
                v_landed, vx_used, vx_before, v_ready = value(16 * v + 16), value(v - 2), value(64 * v), value(k + 1)
                at_v, at_k = value(v), value(k)
                if has(x4) and (not isinstance(x4, int) or x4 >= 4):
                    wait(sp, q_psum, x_used)
                    wait(sp, xt_in, x_before)
                    sp.dma_start(xt[:, (j + 1) % 4, :], x_tiles[:, bass.ds(at_x, 1), :].rearrange(
                        "d o t -> d (o t)")).then_inc(xt_in, 16)
                if has(v):
                    wait(sp, v_out, v_landed)
                    wait(sp, pv_done, vx_used)
                    wait(sp, v_in, vx_before)
                    for h in range(KV):
                        sp.dma_start(
                            vx_e[h * C:(h + 1) * C, (j + 1) % 4, :, h, 0:HD],
                            v_scr[bass.ds(at_v, 1)].rearrange("o (c k) e -> k (o c) e", k=C)[:, :, h * HD:(h + 1) * HD],
                        ).then_inc(v_in, 16)
                if has(k):
                    wait(sp, v_copied, v_ready)
                    sp.dma_start(v_scr[bass.ds(at_k, 1)].rearrange("o t e -> t (o e)"),
                                 vn[:, j % 2, :]).then_inc(v_out, 16)
                if isinstance(s, int) and s in (0, 1):
                    sp.wait_ge(s_split, 2 * s + 2)
                    sp.dma_start(raw[:, s, :], wu[:, s * 1024:(s + 1) * 1024]).then_inc(s_raw[2 + s], 16)

            steps(sp, step)
            with sp.Fori(0, NG) as b:
                sp.wait_ge(ln2_ops, b * LN2_OPS + LN2_OPS)
                sp.dma_start(out.rearrange("(t p) d -> p t d", p=P)[:, bass.ds(b * 4, 4), :],
                             z[:, bass.ds(b * 4, 4), :]).then_inc(s_out, 16)
            sp.wait_ge(s_out, 16 * NG)

        @block.gpsimd
        def _(pool):
            pool.memset(kx[:].bitcast(F32), 0.0).then_inc(s_zero, 1)
            pool.memset(vx[:], 0.0).then_inc(s_zero, 1)
            pool.wait_ge(s_zero, 2)
            for h in range(KV):
                pool.memset(vx_e[h * C:(h + 1) * C, :, :, h, HD], 1.0).then_inc(s_ones, 1)
            pool.wait_ge(s_cst, 16 * 7)

            def step(s, j, ln, tr, rt):
                k = s + 2
                if has(k):
                    shape = [96, CH, KV, C]
                    wait(pool, k_lo, k + 1)
                    wait(pool, b_psum, NU * (k - 2))
                    pool.tensor_tensor(
                        kx[0:96, (j + 2) % 4],
                        kt[:].bitcast(F32).rearrange("p (c o k) -> p c o k", c=CH, o=1).broadcast_to(shape),
                        blk[0:96, :].rearrange("p (a v b) -> p a v b", a=1, b=1).broadcast_to(shape),
                        ALU.mult).then_inc(k_spread, 1)
                if isinstance(s, int) and 0 <= s < 4:
                    hi, lo = ((gh, gl), (uh, ul))[s // 2]
                    cols = slice((s % 2) * 1024, (s % 2 + 1) * 1024)
                    pool.wait_ge(s_raw[s], 16)
                    pool.tensor_copy(hi[:, cols], raw[:, s % 2, :]).then_inc(s_split, 1)
                    pool.wait_ge(s_split, 2 * s + 1)
                    pool.tensor_tensor(lo[:, cols], raw[:, s % 2, :], hi[:, cols].bitcast(F32),
                                       ALU.subtract).then_inc(s_split, 1)

                if tr is not None:
                    wait(pool, ln_ops, tr * LN_OPS + LN_OPS)
                    pool.tensor_copy(z[:, bass.ds(tr * 4, 4), :], x1s[:]).then_inc(x1_kept, 1)

            steps(pool, step)

        @block.tensor
        def _(pe):
            kx_cols = kx[:].rearrange("p s c v k -> p (s c v k)")

            def scores_a(a, j, u):
                pa = pA[(j + 1 + u) % 2]
                qs = (j + 1) % 4
                if u == 0:
                    wait(pe, q_lo, a + 1)
                    wait(pe, k_spread, a + 1)
                if u == 1:
                    wait(pe, k_spread, upto(a + 2))
                wait(pe, a_max, NU * a + u - 1)

                def keys(qc, i, i1, at, start):
                    while i < i1:
                        slot = (qs - 1 + i // CH) % 4
                        run = CH - i % CH
                        if slot < 3:
                            run += CH
                        n = min(i1 - i, run)
                        c0 = slot * CH + i % CH
                        mm = pe.matmul(pa[:, at:at + n * QC], q[:, qs, qc * QC:(qc + 1) * QC],
                                       kx_cols[:, c0 * QC:(c0 + n) * QC],
                                       start=start, stop=True, skip_group_check=True)
                        start = False
                        at += n * QC
                        i += n
                    return mm

                if A_UNITS[u] is None:
                    for qc in range(CH):
                        keys(qc, qc + 8, qc + 9, qc * QC, qc == 0)
                    mm = pe.matmul(pa[:], mask[:, ONE_Q, :],
                                   mask[:, A_RIGHT:A_RIGHT + 1, :].broadcast_to([C, CH, P]),
                                   start=False, stop=True, skip_group_check=True)
                else:
                    qc, half = A_UNITS[u]
                    mm = keys(qc, qc + 4 * half, qc + 4 * half + 4, 0, True)
                    if half == 0:
                        mm = pe.matmul(pa[:, 0:QC], mask[:, ONE_Q, :], mask[:, A_LEFT, :],
                                       start=False, stop=True, skip_group_check=True)
                mm.then_inc(a_psum, 1)

            def scores_b(s, j, u):
                bank = pB[(j + u) % 2]
                if u == 0:
                    wait(pe, m_in_q, s + 1)
                wait(pe, exp_done, NU * s + u - 1)

                def keys(i, qa, qb):
                    return pe.matmul(bank[:, qa * QC:qb * QC],
                                     kx[:, (j - 1 + i // CH) % 4, i % CH].rearrange("p v k -> p (v k)"),
                                     q[:, j, qa * QC:qb * QC], start=(i == u), stop=True, skip_group_check=True)

                def edge(which, qc):
                    return pe.matmul(bank[:, qc * QC:(qc + 1) * QC], mask[:, ONE_K, :], mask[:, which, :],
                                     start=False, stop=True, skip_group_check=True)

                mm = keys(u, 0, min(u + 1, CH))
                if u + 1 < CH:
                    keys(u + NU, u + 1, CH)
                if u < CH:
                    mm = edge(B_LEFT, u)
                if u + 1 < CH:
                    mm = edge(B_RIGHT, u + 1)
                if u == NU - 1:
                    mm = edge(B_RIGHT, 0)
                mm.then_inc(b_psum, 1)

            PV = [[(0, 0, 1, 0), (0, 1, 2, NU)] + [(u, 0, 2, u) for u in range(1, NU)],
                  [(0, 2, 4, NU), (1, 2, 4, 1 + NU), (2, 2, 3, 2), (2, 3, 4, 2 + NU)]
                  + [(u, 2, 4, u) for u in range(3, NU)]]

            def values(p, j, first, last):
                for n in range(first, last):
                    if n == 0:
                        wait(pe, exp_done, NU * p + NU)
                        v_tiles = upto(p + 2)
                        wait(pe, v_in, v_tiles * 64)
                        wait(pe, oT_done, p)
                    for half in range(2):
                        u, qa, qb, i = PV[half][n]
                        mm = pe.matmul(pO[half * VW:(half + 1) * VW, (qa - 2 * half) * QC:(qb - 2 * half) * QC],
                                       vx[:, (j - 2 + i // CH) % 4, i % CH, :],
                                       probs[:, (j - 1) % 2, u, qa * QC:qb * QC],
                                       start=(n == 0), stop=(n == len(PV[0]) - 1), skip_group_check=True)
                if last == len(PV[0]):
                    mm.then_inc(pv_done, 1)

            share = [0, 0, 2, 3, 4, 5, 6, 7, 8, len(PV[0])]

            def step(s, j, ln, tr, rt):
                k = s + 2
                if s == FIRST if isinstance(s, int) else False:
                    pe.wait_ge(s_cst, 16 * 7)
                    pe.wait_ge(s_x0, 16)
                    pe.wait_ge(s_ones, KV)
                    pe.wait_ge(s_const, 2)
                if has(k):
                    xk = xt[:, (j + 2) % 4, :]
                    if not isinstance(k, int) or k >= 4:
                        wait(pe, xt_in, 16 * (k - 3))
                    wait(pe, v_copied, k)
                    wait(pe, z_done, s - 3)
                    wait(pe, attT_done, s - 2)
                    pe.matmul(pW[0:96, 0:P], wk_sb[:], xk, start=True, stop=True, skip_group_check=True)
                    pe.matmul(pW[:, P:P + KV * HD], xk, wv_sb[:], start=True, stop=True,
                              skip_group_check=True).then_inc(kv_psum, 1)
                    wait(pe, q_lo, k)
                    if rt is not None:
                        wait(pe, x1T_done, rt + 1)
                    for g in range(G):
                        mm = pe.matmul(pQ[:, g * P:(g + 1) * P], wq_sb[:, g, :], xk, start=True, stop=True,
                                       skip_group_check=True)
                    mm.then_inc(q_psum, 1)
                if has(s):
                    wait(pe, nm_done, s + 1)
                    wait(pe, m_in_q, s)
                    wait(pe, att_done, s - 2)
                    if rt is not None:
                        wait(pe, rt_ops, rt * RT_OPS + 2)
                    for qc in range(CH):
                        mm = pe.transpose(pM[0:KV, qc * QC:(qc + 1) * QC], nm[:, qc, :], ident)
                    mm.then_inc(m_psum, 1)
                f, w = s - 3, s - 2
                for u in range(NU):
                    if has(w) and u == 2:
                        wait(pe, oT_done, w + 1)
                        wait(pe, m_in_q, upto(s + 1))
                        wait(pe, att_done, w)
                        if rt is not None:
                            wait(pe, rt_ops, rt * RT_OPS + 2)
                    if has(w) and u == 5:
                        wait(pe, att_done, w + 1)
                        wait(pe, z_done, w)
                        wait(pe, v_copied, upto(k + 1))
                    if has(s + 1):
                        scores_a(s + 1, j, u)
                    if has(s):
                        scores_b(s, j, u)
                    if has(s - 1) and share[u] < share[u + 1]:
                        values(s - 1, j, share[u], share[u + 1])
                    if has(f) and u == 1:
                        wait(pe, attT_done, f + 1)
                        wait(pe, v_copied, upto(k + 1))
                        pe.matmul(pW[:, 384:512], attT[:], wo_sb[:], start=True, stop=True,
                                  skip_group_check=True).then_inc(y_psum, 1)
                    if has(w) and u == 2:
                        for g in range(G):
                            mm = pe.transpose(pM[0:P // 2, g * P:(g + 1) * P], oT[:, g::G], ident)
                        mm.then_inc(o_psum, 1)
                    if has(w) and u == 5:
                        for half in range(2):
                            mm = pe.transpose(pW[:, 256 + half * 64:320 + half * 64],
                                              att[:, half].rearrange("p g v d -> p (g v d)"), ident[0:64, 0:64])
                        mm.then_inc(attT_psum, 1)
                    if tr is not None and u == 3:
                        wait(pe, ln_ops, tr * LN_OPS + LN_OPS)
                        wait(pe, q_lo, upto(s + 3))
                        for t in range(4):
                            mm = pe.transpose(pQ[:, t * P:(t + 1) * P], x1s[:, t, :], ident)
                        mm.then_inc(x1T_psum, 1)
                    if tr is not None and u == 6:
                        wait(pe, x1T_done, tr + 1)
                        wait(pe, m_in_q, upto(s + 1))
                        wait(pe, att_done, upto(s - 1))
                        for t in range(4):
                            mm = pe.matmul(pM[:, t * E:(t + 1) * E], x1T[:, t * P:(t + 1) * P], wr_sb[:],
                                           start=True, stop=True, skip_group_check=True)
                        mm.then_inc(lg_psum, 1)

            steps(pe, step)

            pe.wait_ge(s_split, 8)
            pe.wait_ge(s_wd, 16)
            pe.wait_ge(a_max, NU * NT)
            pe.wait_ge(exp_done, NU * NT)
            pe.wait_ge(z_done, NT)
            pe.wait_ge(x1T_done, NG)

            def gate_up(b, n):
                cols = slice(n * P, (n + 1) * P)
                xs = bass.ds(b * TC, TC)

                def product(bank, hi, lo):
                    pe.matmul(bank[:], hi[:, cols], x1h[:, xs], start=True, stop=False)
                    pe.matmul(bank[:], hi[:, cols], x1l[:, xs], start=False, stop=False)
                    return pe.matmul(bank[:], lo[:, cols], x1h[:, xs], start=False, stop=True)

                wait(pe, sg_done, b * NH + (n - 1))
                wait(pe, h_done, b * NH + (n - 1))
                product(pA[n % 2], gh, gl).then_inc(g_psum, 1)
                product(pB[n % 2], uh, ul).then_inc(u_psum, 1)

            def down(b, e):
                bank = (pW, pQ)[e % 2]
                wait(pe, h_done, b * NH + (FH * e + FH))
                wait(pe, acc_done, b * E + (e - 1))
                for t in range(4):
                    for f in range(FH):
                        n = FH * e + f
                        mm = pe.matmul(bank[:, t * P:(t + 1) * P], hid[:, n % 4, t * P:(t + 1) * P],
                                       wd_sb[:, n, :], start=(f == 0), stop=(f == FH - 1), skip_group_check=True)
                mm.then_inc(d_psum, 1)

            def experts(b, before):
                wait(pe, x1l_done, b + 1)
                for n in range(NH):
                    gate_up(b, n)
                    if n % 2 and n >= 3:
                        down(b, (n - 3) // 2)
                    if n == 1 and before is not None:
                        down(before, E - 1)

            experts(0, None)
            with pe.Fori(1, NG) as b:
                experts(b, b - 1)
            down(NG - 1, E - 1)

        @block.scalar
        def _(act):
            act.wait_ge(s_cst, 16 * 7)
            act.wait_ge(s_kxr, 16)
            act.wait_ge(s_zero, 2)
            act.copy(mask[:].rearrange("p a b -> p (a b)"), cst[0:C, C_MASK:C_END]).then_inc(s_const, 1)
            act.copy(kx[96:P].rearrange("p s c v k -> p (s c v k)"),
                     probs[96:P, 1, 0:4, :].rearrange("p a b -> p (a b)")).then_inc(s_const, 1)
            act.wait_ge(s_const, 2)

            def step(s, j, ln, tr, rt):
                k = s + 2
                if has(k):
                    wait(act, kv_psum, k + 1)
                    wait(act, k_spread, k)
                    act.activation(kt[:], pW[0:96, 0:P], ACT.Copy).then_inc(k_hi, 1)
                    wait(act, q_psum, k + 1)
                    wait(act, b_psum, NU * (k - 3))
                    act.activation(q[:, (j + 2) % 4, :].rearrange("p (t g) -> p g t", g=G),
                                   pQ[:].rearrange("p (g t) -> p g t", g=G), ACT.Identity,
                                   bias=cst[:, bass.ds(k + C_FLAG, 1)], scale=SCALE).then_inc(q_hi, 1)
                if has(s):
                    wait(act, m_psum, s + 1)
                    act.activation(q[96:96 + KV, j, :], pM[0:KV, :], ACT.Copy).then_inc(m_in_q, 1)
                w = s - 2
                if has(w):
                    wait(act, pv_done, w + 1)
                    wait(act, o_psum, w)
                    act.copy(oT[:], pO[:, 0:2 * QC]).then_inc(oT_done, 1)
                for u in range(NU):
                    if has(s):
                        wait(act, b_psum, NU * s + u + 1)
                        if u == 0:
                            wait(act, pv_done, s - 1)
                        act.activation(probs[:, j % 2, u, :], pB[(j + u) % 2][:], ACT.Exp).then_inc(exp_done, 1)
                    if has(w) and u == 6:
                        wait(act, attT_psum, w + 1)
                        wait(act, y_psum, w)
                        act.copy(attT[:], pW[:, 256:384]).then_inc(attT_done, 1)
                    if tr is not None and u == 3:
                        wait(act, x1T_psum, tr + 1)
                        wait(act, lg_psum, tr)
                        wait(act, x1l_done, tr)
                        act.copy(x1T[:], pQ[:]).then_inc(x1T_done, 1)
                        wait(act, x1T_done, tr + 1)
                        act.copy(x1h[:, bass.ds(tr * TC, TC)], x1T[:]).then_inc(x1h_done, 1)
                    if rt is not None and u == 0:
                        wait(act, rt_ops, rt * RT_OPS + 2)
                        act.activation(rt_v(1), rt_v(0), ACT.Exp).then_inc(rt_exp, 1)
                    if rt is not None and u == 6:
                        wait(act, rt_ops, rt * RT_OPS + 17)
                        act.activation(rs[:, 7, :], rs[:, 6, :], ACT.Exp).then_inc(rt_exp, 1)

            steps(act, step)
            act.wait_ge(pv_done, NT)

            with act.Fori(0, NG) as b:
                for n in range(NH):
                    act.wait_ge(g_psum, b * NH + (n + 1))
                    act.activation(sg[:, n % 2, :], pA[n % 2][:], ACT.Silu).then_inc(sg_done, 1)

        @block.vector
        def _(dve):
            def rsqrt_op(n, var, sem_inc):
                a, y, h = nw[:, 0, :], nw[:, 1, :], nw[:, 2, :]
                if n == 0:
                    op = dve.tensor_scalar(a, var, EPS, None, ALU.add)
                elif n == 1:
                    op = dve.tensor_scalar(y.bitcast(I32), a.bitcast(I32), -0.5, float(RSQRT_SEED),
                                           ALU.mult, ALU.add)
                elif n % 3 == 2:
                    op = dve.scalar_tensor_tensor(h, y, -0.5, y, ALU.mult, ALU.mult)
                elif n % 3 == 0:
                    op = dve.tensor_tensor(h, h, a, ALU.mult)
                else:
                    op = dve.scalar_tensor_tensor(y, h, 1.5, y, ALU.add, ALU.mult)
                op.then_inc(sem_inc, 1)

            def normalise(dst, t, i, sem_inc):
                dve.tensor_scalar(dst, tile(t), mv[:, i, 0:1], nw[:, 1, i:i + 1], ALU.subtract,
                                  ALU.mult).then_inc(sem_inc, 1)

            def tile(t):
                return z[:, bass.ds(t, 1), :].rearrange("p o d -> p (o d)")

            def ln_op(g, n):
                if n == 0:
                    wait(dve, mv_done, g * 4 + 4)
                wait(dve, ln_ops, g * LN_OPS + n)
                if n < 11:
                    rsqrt_op(n, mv[:, :, 1], ln_ops)
                else:
                    if n == 11:
                        wait(dve, x1_kept, g)
                        wait(dve, x1T_psum, g)
                    normalise(x1s[:, n - 11, :], g * 4 + (n - 11), n - 11, ln_ops)

            def each(v):
                return v.rearrange("p (t o) -> p t o", o=1).broadcast_to([P, 4, E])

            def rt_op(g, n):
                lg = pM[:, 0:4 * E].rearrange("p (t e) -> p t e", e=E)
                ls, ex, pr, eq, key, one1, one2, p2 = (rt_v(i) for i in range(8))
                mx, sm, ri, m1, km, m2, dm, e2, den, w1, w2 = (rs[:, i, :] for i in range(11))
                rev = cst[:, C_REV:C_REV + E].rearrange("p (o e) -> p o e", o=1).broadcast_to([P, 4, E])
                if n == 0:
                    wait(dve, lg_psum, g + 1)
                if n == 2:
                    wait(dve, rt_exp, g * 2 + 1)
                if n == 17:
                    wait(dve, rt_exp, g * 2 + 2)
                wait(dve, rt_ops, g * RT_OPS + n)

                def largest(dst, src):
                    return dve.tensor_reduce(dst, src, AX.X, ALU.max)

                if n == 0:
                    op = largest(mx, lg)
                elif n == 1:
                    op = dve.tensor_tensor(ls, lg, each(mx), ALU.subtract)
                elif n == 2:
                    op = dve.tensor_reduce(sm, ex, AX.X, ALU.add)
                elif n == 3:
                    op = dve.reciprocal(ri, sm)
                elif n == 4:
                    op = dve.tensor_tensor(pr, ex, each(ri), ALU.mult)
                elif n == 5:
                    op = largest(m1, pr)
                elif n == 6:
                    op = dve.tensor_tensor(eq, pr, each(m1), ALU.is_equal)
                elif n == 7:
                    op = dve.tensor_tensor(key, eq, rev, ALU.mult)
                elif n == 8:
                    op = largest(km, key)
                elif n == 9:
                    op = dve.tensor_tensor(one1, key, each(km), ALU.is_equal)
                elif n == 10:
                    op = dve.scalar_tensor_tensor(p2, one1, -2.0, pr, ALU.mult, ALU.add)
                elif n == 11:
                    op = largest(m2, p2)
                elif n == 12:
                    op = dve.tensor_tensor(eq, p2, each(m2), ALU.is_equal)
                elif n == 13:
                    op = dve.tensor_tensor(key, eq, rev, ALU.mult)
                elif n == 14:
                    op = largest(km, key)
                elif n == 15:
                    op = dve.tensor_tensor(one2, key, each(km), ALU.is_equal)
                elif n == 16:
                    op = dve.tensor_tensor(dm, m2, m1, ALU.subtract)
                elif n == 17:
                    op = dve.tensor_scalar(den, e2, 1.0, None, ALU.add)
                elif n == 18:
                    op = dve.reciprocal(w1, den)
                elif n == 19:
                    op = dve.tensor_tensor(w2, e2, w1, ALU.mult)
                elif n == 20:
                    op = dve.tensor_tensor(one1, one1, each(w1), ALU.mult)
                elif n == 21:
                    op = dve.tensor_tensor(one2, one2, each(w2), ALU.mult)
                else:
                    op = dve.tensor_tensor(wt[:, bass.ds(g * 4, 4), :], one1, one2, ALU.add)
                op.then_inc(rt_ops, 1)

            dve.wait_ge(s_z, 16)

            def step(s, j, ln, tr, rt):
                k = s + 2
                if has(k):
                    wait(dve, k_hi, k + 1)
                    dve.tensor_tensor(kt[64:96, :], pW[64:96, 0:P], kt[64:96, :].bitcast(F32),
                                      ALU.subtract).then_inc(k_lo, 1)
                    wait(dve, v_out, 16 * (k - 1))
                    dve.tensor_copy(vn[:, j % 2, :], pW[:, P:P + KV * HD]).then_inc(v_copied, 1)
                    wait(dve, q_hi, k + 1)
                    ql = q[32:64, (j + 2) % 4, :].rearrange("p (t g) -> p g t", g=G)
                    dve.scalar_tensor_tensor(ql, pQ[32:64, :].rearrange("p (g t) -> p g t", g=G), SCALE,
                                             ql.bitcast(F32), ALU.mult, ALU.subtract).then_inc(q_lo, 1)
                a = s + 1
                f, w = s - 3, s - 2
                for u in range(NU):
                    if has(f) and u == 4:
                        wait(dve, z_done, f + 1)
                    if has(f) and u == 5:
                        wait(dve, st_done, f + 1)
                    if has(a):
                        pa = pA[(j + 1 + u) % 2]
                        wait(dve, a_psum, NU * a + u + 1)
                        if u == 0:
                            wait(dve, nm_done, a)
                        if A_UNITS[u] is None:
                            dve.tensor_reduce(mp[:, 2], pa[:].rearrange("p (c v k) -> p c v k", c=CH, v=KV),
                                              AX.X, ALU.max).then_inc(a_max, 1)
                        else:
                            qc, half = A_UNITS[u]
                            dve.tensor_reduce(mp[:, half, qc], pa[:].rearrange("p (i v k) -> p v i k", v=KV, k=C),
                                              AX.XY, ALU.max).then_inc(a_max, 1)
                    if has(w) and u == 2:
                        o = pM[0:P // 2, :].rearrange("p (g h e) -> p g h e", g=G, h=2)
                        wait(dve, o_psum, w + 1)
                        wait(dve, att_done, w)
                        dve.reciprocal(rden[:], o[:, :, :, HD:KV * (HD + 1):HD + 1]).then_inc(den_done, 1)
                    if has(w) and u == 3:
                        o = pM[0:P // 2, :].rearrange("p (g h e) -> p g h e", g=G, h=2)[:, :, :, 0:KV * (HD + 1)]
                        wait(dve, den_done, w + 1)
                        wait(dve, attT_psum, w)
                        dve.tensor_tensor(
                            att[:].rearrange("p h g v d -> p g h v d"),
                            o.rearrange("p g h (v e) -> p g h v e", v=KV)[:, :, :, :, 0:HD],
                            rden[:].rearrange("p g h (v o) -> p g h v o", o=1).broadcast_to([P // 2, G, 2, KV, HD]),
                            ALU.mult).then_inc(att_done, 1)
                    if ln is not None and u < 8:
                        for n in range(2 * u, min(2 * u + 2, LN_OPS)):
                            ln_op(ln, n)
                    if rt is not None:
                        for n in range(2 + (7 * u + 2) // 3, 2 + (7 * (u + 1) + 2) // 3):
                            if n < RT_OPS:
                                rt_op(rt, n)
                    if tr is not None and u == 5:
                        wait(dve, x1h_done, tr + 1)
                        dve.tensor_tensor(x1l[:, bass.ds(tr * TC, TC)], x1T[:],
                                          x1h[:, bass.ds(tr * TC, TC)].bitcast(F32), ALU.subtract).then_inc(x1l_done, 1)
                    if tr is not None and u == 7:
                        rt_op(tr, 0)
                        rt_op(tr, 1)
                    if has(f) and u == 2:
                        wait(dve, y_psum, f + 1)
                        dve.tensor_tensor(tile(f), pW[:, 384:512], tile(f), ALU.add).then_inc(z_done, 1)
                    if has(f) and u == 4:
                        dve.bn_stats(st6[:, (j - 3) % 4, :], tile(f)).then_inc(st_done, 1)
                    if has(f) and u == 8:
                        dve.bn_aggr(mv[:, (j - 3) % 4, :], st6[:, (j - 3) % 4, :]).then_inc(mv_done, 1)
                if has(a):
                    wait(dve, a_max, NU * a + NU)
                    wait(dve, m_psum, a)
                    dve.tensor_reduce(nm[:], mp[:].rearrange("p n c v -> p c v n"), AX.X, ALU.max,
                                      negate=True).then_inc(nm_done, 1)

            steps(dve, step)
            dve.wait_ge(pv_done, NT)
            dve.wait_ge(x1_kept, NG)

            def hidden(b, n):
                dve.wait_ge(sg_done, b * NH + (n + 1))
                dve.wait_ge(u_psum, b * NH + (n + 1))
                wait(dve, d_psum, b * E + ((n - 4) // 2 + 1))
                dve.tensor_tensor(hid[:, n % 4, :], sg[:, n % 2, :], pB[n % 2][:], ALU.mult).then_inc(h_done, 1)

            def accumulate(b, e):
                bank = (pW, pQ)[e % 2]
                dve.wait_ge(d_psum, b * E + (e + 1))
                wait(dve, acc_done, b * E + e)
                for t in range(4):
                    op = dve.scalar_tensor_tensor(
                        tile(b * 4 + t), bank[:, t * P:(t + 1) * P],
                        wt[:, bass.ds(b * 4 + t, 1), e], tile(b * 4 + t), ALU.mult, ALU.add)
                op.then_inc(acc_done, 1)

            def ln2_op(b, n):
                if n >= 8:
                    wait(dve, ln2_ops, b * LN2_OPS + n)
                if n < 4:
                    dve.bn_stats(st6[:, n, :], tile(b * 4 + n)).then_inc(ln2_ops, 1)
                elif n < 8:
                    dve.bn_aggr(mv[:, n - 4, :], st6[:, n - 4, :]).then_inc(ln2_ops, 1)
                elif n < 19:
                    rsqrt_op(n - 8, mv[:, :, 1], ln2_ops)
                else:
                    normalise(tile(b * 4 + (n - 19)), b * 4 + (n - 19), n - 19, ln2_ops)

            def experts(b, before):
                for n in range(NH):
                    if before is not None and n == 3:
                        dve.wait_ge(acc_done, before * E + E)
                    if before is not None and n == 4:
                        dve.wait_ge(ln2_ops, before * LN2_OPS + 4)
                    hidden(b, n)
                    if n >= 4 and n % 2 == 0:
                        accumulate(b, (n - 4) // 2)
                    if before is not None and n in (0, 2):
                        accumulate(before, E - 2 + n // 2)
                    if before is not None and n >= 3:
                        first, last = ((0, 4), (4, 8))[n - 3] if n < 5 else (2 * n - 2, 2 * n)
                        for i in range(first, min(last, LN2_OPS)):
                            ln2_op(before, i)

            experts(0, None)
            with dve.Fori(1, NG) as b:
                experts(b, b - 1)
            accumulate(NG - 1, E - 2)
            accumulate(NG - 1, E - 1)
            for n in range(LN2_OPS):
                if n == 0:
                    dve.wait_ge(acc_done, NG * E)
                if n == 4:
                    dve.wait_ge(ln2_ops, (NG - 1) * LN2_OPS + 4)
                ln2_op(NG - 1, n)


def constants():
    cst = np.zeros((P, C_END), np.float32)
    cst[:, C_ID:C_ID + P] = np.eye(P)
    for slot in range(4):
        for t in range(NT):
            j = t % 4
            outside = (t % TPS == 0 and slot == (j - 1) % 4) or (t % TPS == TPS - 1 and slot == (j + 1) % 4)
            cst[100 + slot, C_FLAG + t] = -BIG if outside else 0.0
    cst[:, C_REV:C_REV + E] = np.arange(E, 0, -1)
    m = cst[0:C, C_MASK:C_END].reshape(C, 6, P)
    row = np.arange(C)[:, None]
    tok_g = np.arange(P)[None, :] // G
    v_tok = np.arange(P)[None, :] % C
    m[:, ONE_Q] = row == tok_g
    m[:, A_LEFT] = np.where(v_tok < row, -BIG, 0.0)
    m[:, A_RIGHT] = np.where(v_tok > row, -BIG, 0.0)
    m[:, ONE_K] = row == v_tok
    m[:, B_LEFT] = np.where(row < tok_g, -BIG, 0.0)
    m[:, B_RIGHT] = np.where(row > tok_g, -BIG, 0.0)
    kx_rows = np.zeros((C, 4, CH, KV, C), np.float32)
    for v in range(KV):
        kx_rows[v, :, :, v, :] = 1.0
    for slot in range(4):
        kx_rows[4 + slot, slot] = 1.0
    blocks = np.zeros((P, KV), np.float32)
    for r in range(96):
        blocks[r, (r % 32) // HD] = 1.0
    return cst, kx_rows.reshape(C, 4, TC), blocks


def kernel(L0_attn_x, L0_attn_Wq, L0_attn_Wk, L0_attn_Wv, L0_attn_Wo, L0_ffn_kernel_router_DE,
           L0_ffn_kernel_gating_EDF, L0_ffn_kernel_up_EDF, L0_ffn_kernel_down_EFD):
    from concourse import bacc
    from concourse.bass_utils import run_bass_kernel_spmd

    x = np.ascontiguousarray(L0_attn_x).reshape(TOK, D)
    w_q = np.asarray(L0_attn_Wq).reshape(KV, G, HD, D).transpose(3, 1, 0, 2).reshape(D, G, 1, KV * HD)
    wq = np.zeros((D, G, P), np.float32)
    wq[:, :, 0:96] = np.broadcast_to(w_q, (D, G, 3, KV * HD)).reshape(D, G, 96)
    w_k = np.asarray(L0_attn_Wk).T.reshape(D, 1, KV * HD)
    cst, kx_rows, blocks = constants()
    arrays = {
        "x": x,
        "xT": np.ascontiguousarray(x.T),
        "wq": wq,
        "wk": np.ascontiguousarray(np.broadcast_to(w_k, (D, 3, KV * HD)).reshape(D, 96)),
        "wv": np.ascontiguousarray(np.asarray(L0_attn_Wv).T),
        "wo": np.ascontiguousarray(np.asarray(L0_attn_Wo).reshape(D, KV, G, HD).transpose(2, 1, 3, 0).reshape(P, D)),
        "wr": np.ascontiguousarray(L0_ffn_kernel_router_DE),
        "wg": np.ascontiguousarray(np.asarray(L0_ffn_kernel_gating_EDF).transpose(1, 0, 2).reshape(D, E * F)),
        "wu": np.ascontiguousarray(np.asarray(L0_ffn_kernel_up_EDF).transpose(1, 0, 2).reshape(D, E * F)),
        "wd": np.ascontiguousarray(
            np.asarray(L0_ffn_kernel_down_EFD).reshape(E * FH, P, D).transpose(1, 0, 2)),
        "consts": cst,
        "kx_rows": kx_rows,
        "blocks": blocks,
    }
    nc = bacc.Bacc("TRN2", target_bir_lowering=False, num_devices=1)
    ins = [nc.dram_tensor(n, a.shape, mybir.dt.from_np(a.dtype), kind="ExternalInput").ap() for n, a in arrays.items()]
    out = nc.dram_tensor("out", (TOK, D), F32, kind="ExternalOutput").ap()
    v_scr = nc.dram_tensor("v_scr", (NT, P, KV * HD), F32, kind="Internal").ap()
    attention_moe(nc, *ins, out, v_scr)
    r = run_bass_kernel_spmd(nc, [arrays], core_ids=[0])
    return r.results[0]["out"].reshape(NB, SEQ, D)
```

```python
from contextlib import ExitStack

import numpy as np

import concourse.bass as bass
from concourse import mybir

F32 = mybir.dt.float32
F32R = mybir.dt.float32r
BF16 = mybir.dt.bfloat16
I32 = mybir.dt.int32
ALU = mybir.AluOpType
ACT = mybir.ActivationFunctionType
AX = mybir.AxisListType

P = 128
D = 128
SEQ = 2048
NB = 2
TOK = NB * SEQ
NT = TOK // P
TPS = SEQ // P
KV, G, HD = 4, 4, 8
C = 32
CH = P // C
VW = KV * HD
QC = P
TC = CH * QC
NU = 9
SUMS = NU - 1
E, F = 8, 256
FH = F // P
SCALE = 1.0 / float(np.sqrt(np.float32(HD)))
BIG = 1e30
EPS = 1e-5
NG = NT // 4
NH = E * FH
LN_OPS = 15
LN2_OPS = 23
RT_OPS = 23
RSQRT_SEED = 0x5F3759DF

C_ID, C_FLAG, C_REV, C_MASK = 0, P, P + NT, P + NT + E
C_ONES = C_MASK + 6 * P
C_ADD = C_ONES + KV
C_END = C_ADD + 2 * VW
O_AT, DEN_AT = P, 3 * P
ONE_Q, A_LEFT, A_RIGHT, ONE_K, B_LEFT, B_RIGHT, BLOCK = 0, 1, 2, 3, 4, 5, 6

A_UNITS = [(0, 0), (0, 1), (1, 0), (2, 0), (3, 0), (1, 1), (2, 1), (3, 1), None]


def attention_moe(nc, x, xT, wq, wk, wv, wo, wr, wg, wu, wd, consts, kx_rows, blocks, out, v_scr):
    with ExitStack() as ctx:
        def sb(name, shape, dt=F32):
            return ctx.enter_context(nc.sbuf_tensor(name, shape, dt))

        def pb(name):
            return ctx.enter_context(nc.psum_tensor(name, [P, 512], F32))

        def sem(name):
            return ctx.enter_context(nc.semaphore(name))

        cst = sb("cst", [P, C_END])
        blk = sb("blk", [P, KV])
        ident = cst[:, C_ID:C_ID + P]
        mask = sb("mask", [C, 6, P], BF16)
        wq_sb = sb("wq_sb", [P, G, P])
        wk_sb = sb("wk_sb", [P, 96])
        wv_sb = sb("wv_sb", [P, KV * HD])
        wo_sb = sb("wo_sb", [P, D])
        wr_sb = sb("wr_sb", [P, E])
        xt = sb("xt", [P, 4, P])
        z = sb("z", [P, NT, D])
        x1h = sb("x1h", [P, TOK], F32R)
        x1l = sb("x1l", [P, TOK], F32R)
        q = sb("q", [P, 4, TC], F32R)
        kt = sb("kt", [96, P], F32R)
        kx = sb("kx", [P, 4, CH, KV, C], F32R)
        vn = sb("vn", [P, 2, KV * HD])
        vx = sb("vx", [P, 4, CH, VW])
        vx_e = vx[:].rearrange("p s c (v e) -> p s c v e", v=KV)
        probs = sb("probs", [P, 2, NU, TC])
        mp = sb("mp", [P, 3, CH, KV])
        nm = sb("nm", [P, CH, C])
        psums = sb("psums", [P, 2, 2, TC])
        oT = sb("oT", [P, 2 * QC])
        rden = sb("rden", [P // 2, G, 2, KV])
        att = sb("att", [P // 2, 2, G, KV, HD])
        attT = sb("attT", [P, P])
        st6 = sb("st6", [P, 4, 6])
        mv = sb("mv", [P, 4, 2])
        nw = sb("nw", [P, 4, 4])
        x1s = sb("x1s", [P, 4, D])
        x1T = sb("x1T", [P, TC])
        rt = sb("rt", [P, 8, 4, E])
        rs = sb("rs", [P, 12, 4])
        wt = sb("wt", [P, NT, E])
        raw = sb("raw", [P, 2, 1024])
        gh = sb("gh", [P, E * F], F32R)
        gl = sb("gl", [P, E * F], F32R)
        uh = sb("uh", [P, E * F], F32R)
        ul = sb("ul", [P, E * F], F32R)
        wd_sb = sb("wd_sb", [P, NH, D])
        sg = probs[:, 0, 0:2, :]
        hid = probs[:, 0, 2:6, :]

        def rt_v(i):
            return rt[:, i]

        pA = [pb("pA0"), pb("pA1")]
        pB = [pb("pB0"), pb("pB1")]
        pW = pb("pW")
        pQ = pb("pQ")
        pM = pb("pM")
        pO = pb("pO")

        s_proj = sem("s_proj")
        s_cst = sem("s_cst")
        s_wts = sem("s_wts")
        s_z = sem("s_z")
        s_kxr = sem("s_kxr")
        s_zero = sem("s_zero")
        s_const = sem("s_const")
        s_raw = [sem(f"s_raw{i}") for i in range(4)]
        s_wd = sem("s_wd")
        s_hi = sem("s_hi")
        s_lo = sem("s_lo")
        xt_in = sem("xt_in")
        kv_psum = sem("kv_psum")
        q_psum = sem("q_psum")
        k_hi = sem("k_hi")
        k_lo = sem("k_lo")
        v_copied = sem("v_copied")
        q_hi = sem("q_hi")
        q_lo = sem("q_lo")
        k_spread = sem("k_spread")
        v_out = sem("v_out")
        v_in = sem("v_in")
        a_psum = sem("a_psum")
        a_max = sem("a_max")
        nm_done = sem("nm_done")
        m_psum = sem("m_psum")
        m_in_q = sem("m_in_q")
        b_psum = sem("b_psum")
        exp_done = sem("exp_done")
        pv_done = sem("pv_done")
        sum_ops = sem("sum_ops")
        den_psum = sem("den_psum")
        den_done = sem("den_done")
        oT_done = sem("oT_done")
        o_psum = sem("o_psum")
        att_done = sem("att_done")
        attT_psum = sem("attT_psum")
        attT_done = sem("attT_done")
        y_psum = sem("y_psum")
        z_done = sem("z_done")
        st_done = sem("st_done")
        mv_done = sem("mv_done")
        ln_ops = sem("ln_ops")
        x1_kept = sem("x1_kept")
        x1T_psum = sem("x1T_psum")
        x1T_done = sem("x1T_done")
        x1h_done = sem("x1h_done")
        x1l_done = sem("x1l_done")
        lg_psum = sem("lg_psum")
        rt_ops = sem("rt_ops")
        rt_exp = sem("rt_exp")
        g_psum = sem("g_psum")
        u_psum = sem("u_psum")
        sg_done = sem("sg_done")
        h_done = sem("h_done")
        d_psum = sem("d_psum")
        acc_done = sem("acc_done")
        ln2_ops = sem("ln2_ops")
        s_out = sem("s_out")

        def has(t):
            return not isinstance(t, int) or 0 <= t < NT

        def wait(eng, s, n):
            if not isinstance(n, int) or n > 0:
                eng.wait_ge(s, n)

        def upto(n):
            return min(n, NT) if isinstance(n, int) else n

        FIRST, LOOP0, LOOPS = -2, 6, 5
        TAIL = {0: NT, 1: NT + 1, 2: NT + 2, 6: NT + 3, 8: NT + 4, 10: NT + 5}

        def one(step, s):
            def group(c):
                n = (s - c) // 4
                return n if (s - c) % 4 == 0 and 0 <= n < NG else None

            step(s, s % 4, group(6), group(7), group(8), group(9))

        def steps(eng, step):
            for s in range(FIRST, LOOP0):
                one(step, s)
            with eng.Fori(1, 1 + LOOPS) as it:
                for c in range(2, 6):
                    step(it * 4 + c, c % 4, it - 1 if c == 2 else None, it - 1 if c == 3 else None,
                         it - 1 if c == 4 else None, it - 1 if c == 5 else None)
            for s in range(LOOP0 + 4 * LOOPS, NT):
                one(step, s)

        block = ctx.enter_context(nc.Block())

        @block.sync
        def _(sp):
            for dst, src in ((wk_sb[:], wk), (xt[:].rearrange("p s t -> p (s t)"), xT[:, 0:4 * P]), (wv_sb[:], wv),
                             (wq_sb[:], wq)):
                sp.dma_start(dst, src).then_inc(s_proj, 16)
            sp.dma_start(cst[:], consts).then_inc(s_cst, 16)
            sp.dma_start(probs[96:P, 1, 0:4, :], kx_rows).then_inc(s_kxr, 16)
            sp.dma_start(blk[:], blocks).then_inc(s_cst, 16)
            sp.dma_start(wo_sb[:], wo).then_inc(s_wts, 16)
            sp.dma_start(wr_sb[:], wr).then_inc(s_wts, 16)
            sp.dma_start(z[:], x.rearrange("(t p) d -> p t d", p=P)).then_inc(s_z, 16)
            sp.dma_start(raw[:, 0, :], wg[:, 0:1024]).then_inc(s_raw[0], 16)
            sp.dma_start(raw[:, 1, :], wg[:, 1024:2048]).then_inc(s_raw[1], 16)
            sp.dma_start(wd_sb[:], wd).then_inc(s_wd, 16)
            sp.wait_ge(s_zero, 2)

            x_tiles = xT.rearrange("d (n t) -> d n t", t=P)

            def value(n):
                return n if isinstance(n, int) else sp.snap(sp.to_reg(n))

            def step(s, j, ln, tr, rt, ru):
                x4, v, k = s + 5, s + 1, s + 2
                x_used, x_before, at_x = value(s + 2), value(16 * (x4 - 4)), value(x4)
                v_landed, vx_used, vx_before, v_ready = value(16 * v + 16), value(v - 2), value(64 * v), value(k + 1)
                at_v, at_k = value(v), value(k)
                if has(x4) and (not isinstance(x4, int) or x4 >= 4):
                    wait(sp, q_psum, x_used)
                    wait(sp, xt_in, x_before)
                    sp.dma_start(xt[:, (j + 1) % 4, :], x_tiles[:, bass.ds(at_x, 1), :].rearrange(
                        "d o t -> d (o t)")).then_inc(xt_in, 16)
                if has(v):
                    wait(sp, v_out, v_landed)
                    wait(sp, pv_done, vx_used)
                    wait(sp, v_in, vx_before)
                    for h in range(KV):
                        sp.dma_start(
                            vx_e[h * C:(h + 1) * C, (j + 1) % 4, :, h, 0:HD],
                            v_scr[bass.ds(at_v, 1)].rearrange("o (c k) e -> k (o c) e", k=C)[:, :, h * HD:(h + 1) * HD],
                        ).then_inc(v_in, 16)
                if has(k):
                    wait(sp, v_copied, v_ready)
                    sp.dma_start(v_scr[bass.ds(at_k, 1)].rearrange("o t e -> t (o e)"),
                                 vn[:, j % 2, :]).then_inc(v_out, 16)
                if isinstance(s, int) and s in (0, 1):
                    sp.wait_ge(s_lo, s + 1)
                    sp.dma_start(raw[:, s, :], wu[:, s * 1024:(s + 1) * 1024]).then_inc(s_raw[2 + s], 16)

            steps(sp, step)
            with sp.Fori(0, NG) as b:
                sp.wait_ge(ln2_ops, b * LN2_OPS + LN2_OPS)
                sp.dma_start(out.rearrange("(t p) d -> p t d", p=P)[:, bass.ds(b * 4, 4), :],
                             z[:, bass.ds(b * 4, 4), :]).then_inc(s_out, 16)
            sp.wait_ge(s_out, 16 * NG)

        @block.gpsimd
        def _(pool):
            pool.memset(kx[:].bitcast(F32), 0.0).then_inc(s_zero, 1)
            pool.memset(vx[:], 0.0).then_inc(s_zero, 1)
            pool.memset(nm[:], 0.0).then_inc(s_zero, 1)

            def step(s, j, ln, tr, rt, ru):
                if has(s):
                    sums = psums[:, j % 2]
                    for n in range(SUMS):
                        last = n == SUMS - 1
                        if n == 0:
                            wait(pool, den_psum, s - 1)
                        if n >= 2:
                            wait(pool, sum_ops, SUMS * s + n - (0 if last else 1))
                        if not last:
                            u = 2 * n + 1 if n < 2 else n + 2
                            wait(pool, exp_done, NU * s + u + 1)
                        if last:
                            a, b = sums[:, 0], sums[:, 1]
                        elif n < 2:
                            a, b = probs[:, j % 2, u - 1], probs[:, j % 2, u]
                        else:
                            a, b = sums[:, n % 2], probs[:, j % 2, u]
                        pool.tensor_tensor(sums[:, 0 if last else n % 2], a, b, ALU.add).then_inc(sum_ops, 1)
                if isinstance(s, int) and 0 <= s < 4:
                    hi, lo = ((gh, gl), (uh, ul))[s // 2]
                    cols = slice((s % 2) * 1024, (s % 2 + 1) * 1024)
                    pool.wait_ge(s_hi, s + 1)
                    pool.tensor_tensor(lo[:, cols], raw[:, s % 2, :], hi[:, cols].bitcast(F32),
                                       ALU.subtract).then_inc(s_lo, 1)

                if tr is not None:
                    wait(pool, ln_ops, tr * LN_OPS + LN_OPS)
                    pool.tensor_copy(z[:, bass.ds(tr * 4, 4), :], x1s[:]).then_inc(x1_kept, 1)

            steps(pool, step)
            for s in TAIL.values():
                one(step, s)

        @block.tensor
        def _(pe):
            kx_cols = kx[:].rearrange("p s c v k -> p (s c v k)")

            def scores_a(a, j, u):
                pa = pA[(j + 1 + u) % 2]
                qs = (j + 1) % 4
                if u == 0:
                    wait(pe, q_lo, a + 1)
                    wait(pe, k_spread, a + 1)
                if u == 5:
                    wait(pe, k_spread, upto(a + 2))
                wait(pe, a_max, NU * a + u - 1)

                def keys(qc, i, i1, at, start):
                    while i < i1:
                        slot = (qs - 1 + i // CH) % 4
                        run = CH - i % CH
                        if slot < 3:
                            run += CH
                        n = min(i1 - i, run)
                        c0 = slot * CH + i % CH
                        mm = pe.matmul(pa[:, at:at + n * QC], q[:, qs, qc * QC:(qc + 1) * QC],
                                       kx_cols[:, c0 * QC:(c0 + n) * QC],
                                       start=start, stop=True, skip_group_check=True)
                        start = False
                        at += n * QC
                        i += n
                    return mm

                if A_UNITS[u] is None:
                    for qc in range(CH):
                        keys(qc, qc + 8, qc + 9, qc * QC, qc == 0)
                    mm = pe.matmul(pa[:], mask[:, ONE_Q, :],
                                   mask[:, A_RIGHT:A_RIGHT + 1, :].broadcast_to([C, CH, P]),
                                   start=False, stop=True, skip_group_check=True)
                else:
                    qc, half = A_UNITS[u]
                    mm = keys(qc, qc + 4 * half, qc + 4 * half + 4, 0, True)
                    if half == 0:
                        mm = pe.matmul(pa[:, 0:QC], mask[:, ONE_Q, :], mask[:, A_LEFT, :],
                                       start=False, stop=True, skip_group_check=True)
                mm.then_inc(a_psum, 1)

            def scores_b(s, j, u):
                bank = pB[(j + u) % 2]
                if u == 0:
                    wait(pe, m_in_q, s + 1)
                wait(pe, exp_done, NU * s + u - 1)

                def keys(i, qa, qb):
                    return pe.matmul(bank[:, qa * QC:qb * QC],
                                     kx[:, (j - 1 + i // CH) % 4, i % CH].rearrange("p v k -> p (v k)"),
                                     q[:, j, qa * QC:qb * QC], start=(i == u), stop=True, skip_group_check=True)

                mm = keys(u, 0, min(u + 1, CH))
                if u + 1 < CH:
                    keys(u + NU, u + 1, CH)
                if u < CH:
                    n = min(2, CH - u)
                    mm = pe.matmul(bank[:, u * QC:(u + n) * QC], mask[:, ONE_K, :], mask[:, B_LEFT:B_LEFT + n, :],
                                   start=False, stop=True, skip_group_check=True)
                if u == NU - 1:
                    mm = pe.matmul(bank[:, 0:QC], mask[:, ONE_K, :], mask[:, B_RIGHT, :],
                                   start=False, stop=True, skip_group_check=True)
                mm.then_inc(b_psum, 1)

            PV = [[(0, 0, 1, 0)] + [(u, 0, 2, u) for u in (1, 3, 5, 7)],
                  [(0, 1, 2, NU)] + [(u, 0, 2, u) for u in (2, 4, 6, 8)],
                  [(2, 2, 3, 2), (0, 2, 4, NU)] + [(u, 2, 4, u) for u in (3, 5, 7)],
                  [(2, 3, 4, 2 + NU), (1, 2, 4, 1 + NU)] + [(u, 2, 4, u) for u in (4, 6, 8)]]
            ROUNDS = len(PV[0])

            def values(p, j, n):
                if n == 0:
                    wait(pe, exp_done, NU * p + NU)
                    v_tiles = upto(p + 2)
                    wait(pe, v_in, v_tiles * 64)
                    wait(pe, oT_done, p)
                for i, share in enumerate(PV):
                    u, qa, qb, c = share[n]
                    q0 = 2 * (i // 2)
                    mm = pe.matmul(pO[i * VW:(i + 1) * VW, (qa - q0) * QC:(qb - q0) * QC],
                                   vx[:, (j - 2 + c // CH) % 4, c % CH, :],
                                   probs[:, (j - 1) % 2, u, qa * QC:qb * QC],
                                   start=(n == 0), stop=(n == ROUNDS - 1), skip_group_check=True)
                if n == ROUNDS - 1:
                    mm.then_inc(pv_done, 1)

            VALUES_AT, SUMS_AT = (0, 2, 3, 7, 8), 4

            def step(s, j, ln, tr, rt, ru):
                k = s + 2
                if isinstance(s, int) and s == FIRST + 1:
                    pe.wait_ge(s_const, 2)
                if isinstance(s, int) and s == 2:
                    pe.wait_ge(s_wts, 16 * 2)
                if isinstance(s, int) and s == FIRST:
                    pe.wait_ge(s_proj, 16 * 4)
                if has(k):
                    xk = xt[:, (j + 2) % 4, :]
                    if not isinstance(k, int) or k >= 4:
                        wait(pe, xt_in, 16 * (k - 3))
                    wait(pe, v_copied, k)
                    wait(pe, z_done, s - 2)
                    wait(pe, attT_done, s - 2)
                    pe.matmul(pW[0:96, 0:P], wk_sb[:], xk, start=True, stop=True, skip_group_check=True)
                    pe.matmul(pW[:, P:P + KV * HD], xk, wv_sb[:], start=True, stop=True,
                              skip_group_check=True).then_inc(kv_psum, 1)
                    wait(pe, q_lo, k)
                    if rt is not None:
                        wait(pe, x1T_done, rt + 1)
                for g in range(G):
                    if has(k):
                        mm = pe.matmul(pQ[:, g * P:(g + 1) * P], wq_sb[:, g, :], xk, start=True, stop=True,
                                       skip_group_check=True)
                    if has(s) and g == 1:
                        wait(pe, nm_done, s + 1)
                        wait(pe, m_in_q, s)
                        wait(pe, den_done, s - 1)
                        if rt is not None:
                            wait(pe, rt_ops, rt * RT_OPS + 2)
                        pe.transpose(pM[:, 0:QC], nm[:].rearrange("p c v -> p (c v)"), ident).then_inc(m_psum, 1)
                if has(k):
                    mm.then_inc(q_psum, 1)
                w = s - 2
                for u in range(NU):
                    if has(w) and u == 4:
                        wait(pe, att_done, w + 1)
                        wait(pe, v_copied, upto(k + 1))
                    if has(s + 1):
                        scores_a(s + 1, j, u)
                    if has(s - 1) and u in VALUES_AT:
                        values(s - 1, j, VALUES_AT.index(u))
                    if has(s):
                        scores_b(s, j, u)
                    if has(w) and u == 4:
                        for half in range(2):
                            mm = pe.transpose(pW[:, 256 + half * 64:320 + half * 64],
                                              att[:, half].rearrange("p g v d -> p (g v d)"), ident[0:64, 0:64])
                        mm.then_inc(attT_psum, 1)
                    if has(s - 1) and u == SUMS_AT:
                        wait(pe, sum_ops, SUMS * s)
                        wait(pe, att_done, s - 1)
                        for n in range(2 * G):
                            g, half = n // 2, n % 2
                            mm = pe.matmul(pM[0:64, DEN_AT + n * KV:DEN_AT + (n + 1) * KV],
                                           psums[:, (j - 1) % 2, 0, half * 2 * QC + g:(half + 1) * 2 * QC:G],
                                           cst[:, C_ONES:C_ONES + KV], start=True, stop=True, skip_group_check=True)
                        mm.then_inc(den_psum, 1)
                    if has(w) and u == 1:
                        wait(pe, oT_done, w + 1)
                        wait(pe, m_in_q, upto(s + 1))
                        wait(pe, den_done, w + 1)
                        if rt is not None:
                            wait(pe, rt_ops, rt * RT_OPS + 2)
                        for g in range(G):
                            mm = pe.matmul(pM[0:64, O_AT + g * 64:O_AT + (g + 1) * 64], oT[:, g::G],
                                           cst[:, C_ADD:C_ADD + 64], start=True, stop=True, skip_group_check=True)
                        mm.then_inc(o_psum, 1)
                    if has(w) and u == 6:
                        wait(pe, attT_done, w + 1)
                        pe.matmul(pW[:, 384:512], attT[:], wo_sb[:], start=True, stop=True,
                                  skip_group_check=True).then_inc(y_psum, 1)
                    if tr is not None and u == 3:
                        wait(pe, ln_ops, tr * LN_OPS + LN_OPS)
                        wait(pe, q_lo, upto(s + 3))
                        for t in range(4):
                            mm = pe.transpose(pQ[:, t * P:(t + 1) * P], x1s[:, t, :], ident)
                        mm.then_inc(x1T_psum, 1)
                    if tr is not None and u == 7:
                        wait(pe, x1T_done, tr + 1)
                        wait(pe, m_in_q, upto(s + 1))
                        wait(pe, den_done, upto(s))
                        for t in range(4):
                            mm = pe.matmul(pM[:, t * E:(t + 1) * E], x1T[:, t * P:(t + 1) * P], wr_sb[:],
                                           start=True, stop=True, skip_group_check=True)
                        mm.then_inc(lg_psum, 1)

            steps(pe, step)

            pe.wait_ge(s_lo, 4)
            pe.wait_ge(s_wd, 16)
            pe.wait_ge(a_max, NU * NT)
            pe.wait_ge(exp_done, NU * NT)

            def gate_up(b, n):
                cols = slice(n * P, (n + 1) * P)
                xs = bass.ds(b * TC, TC)

                def product(bank, hi, lo):
                    pe.matmul(bank[:], hi[:, cols], x1h[:, xs], start=True, stop=False)
                    pe.matmul(bank[:], hi[:, cols], x1l[:, xs], start=False, stop=False)
                    return pe.matmul(bank[:], lo[:, cols], x1h[:, xs], start=False, stop=True)

                wait(pe, sg_done, b * NH + (n - 1))
                wait(pe, h_done, b * NH + (n - 1))
                product(pA[n % 2], gh, gl).then_inc(g_psum, 1)
                product(pB[n % 2], uh, ul).then_inc(u_psum, 1)

            def down(b, e):
                bank = (pO, pW)[e % 2]
                if isinstance(b, int) and b == 0 and e < 2:
                    pe.wait_ge(*((oT_done, NT), (z_done, NT))[e])
                wait(pe, h_done, b * NH + (FH * e + FH))
                wait(pe, acc_done, b * E + (e - 1))
                for t in range(4):
                    for f in range(FH):
                        n = FH * e + f
                        mm = pe.matmul(bank[:, t * P:(t + 1) * P], hid[:, n % 4, t * P:(t + 1) * P],
                                       wd_sb[:, n, :], start=(f == 0), stop=(f == FH - 1), skip_group_check=True)
                mm.then_inc(d_psum, 1)

            def experts(b, before):
                wait(pe, x1l_done, b + 1)
                for n in range(NH):
                    if before is None and n in TAIL:
                        one(step, TAIL[n])
                    gate_up(b, n)
                    if n % 2 and n >= 3:
                        down(b, (n - 3) // 2)
                    if n == 1 and before is not None:
                        down(before, E - 1)

            experts(0, None)
            with pe.Fori(1, NG) as b:
                experts(b, b - 1)
            down(NG - 1, E - 1)

        @block.scalar
        def _(act):
            act.wait_ge(s_cst, 16 * 2)
            act.copy(mask[:].rearrange("p a b -> p (a b)"), cst[0:C, C_MASK:C_ONES]).then_inc(s_const, 1)

            def step(s, j, ln, tr, rt, ru):
                k, w = s + 2, s - 2
                if has(w):
                    wait(act, pv_done, w + 1)
                    wait(act, o_psum, w)
                    act.copy(oT[:], pO[:, 0:2 * QC]).then_inc(oT_done, 1)
                if has(k):
                    wait(act, kv_psum, k + 1)
                    wait(act, k_spread, k)
                    act.activation(kt[:], pW[0:96, 0:P], ACT.Copy).then_inc(k_hi, 1)
                if has(s):
                    wait(act, m_psum, s + 1)
                    for qc in range(CH):
                        mc = act.activation(q[96:96 + KV, j, qc * QC:(qc + 1) * QC], pM[qc * C:qc * C + KV, 0:QC],
                                            ACT.Copy)
                    mc.then_inc(m_in_q, 1)
                if has(k):
                    wait(act, q_psum, k + 1)
                    wait(act, b_psum, NU * (k - 3))
                    act.activation(q[:, (j + 2) % 4, :].rearrange("p (t g) -> p g t", g=G),
                                   pQ[:].rearrange("p (g t) -> p g t", g=G), ACT.Identity,
                                   bias=cst[:, bass.ds(k + C_FLAG, 1)], scale=SCALE).then_inc(q_hi, 1)
                for u in range(NU):
                    if has(s):
                        wait(act, b_psum, NU * s + u + 1)
                        if u == 0:
                            wait(act, pv_done, s - 1)
                        act.activation(probs[:, j % 2, u, :], pB[(j + u) % 2][:], ACT.Exp).then_inc(exp_done, 1)
                    if has(k) and u == 1:
                        wait(act, k_lo, k + 1)
                        wait(act, b_psum, NU * (k - 2))
                        for v in range(KV):
                            spread = act.activation(kx[0:96, (j + 2) % 4, :, v, :],
                                                    kt[:].bitcast(F32).rearrange("p (c k) -> p c k", c=CH),
                                                    ACT.Copy, scale=blk[0:96, v:v + 1])
                        spread.then_inc(k_spread, 1)
                    if has(w) and u == 4:
                        wait(act, attT_psum, w + 1)
                        wait(act, y_psum, w)
                        act.copy(attT[:], pW[:, 256:384]).then_inc(attT_done, 1)
                    if isinstance(s, int) and 0 <= s < 4 and u == 4:
                        hi = (gh, uh)[s // 2]
                        act.wait_ge(s_raw[s], 16)
                        act.copy(hi[:, (s % 2) * 1024:(s % 2 + 1) * 1024], raw[:, s % 2, :]).then_inc(s_hi, 1)
                    if tr is not None and u == 3:
                        wait(act, x1T_psum, tr + 1)
                        wait(act, lg_psum, tr)
                        wait(act, x1l_done, tr)
                        act.copy(x1T[:], pQ[:]).then_inc(x1T_done, 1)
                        wait(act, x1T_done, tr + 1)
                        act.copy(x1h[:, bass.ds(tr * TC, TC)], x1T[:]).then_inc(x1h_done, 1)
                    if rt is not None and u == 0:
                        wait(act, rt_ops, rt * RT_OPS + 2)
                        act.activation(rt_v(1), rt_v(0), ACT.Exp).then_inc(rt_exp, 1)
                    if ru is not None and u == 4:
                        wait(act, rt_ops, ru * RT_OPS + 17)
                        act.activation(rs[:, 7, :], rs[:, 6, :], ACT.Exp).then_inc(rt_exp, 1)

            steps(act, step)
            act.wait_ge(pv_done, NT - 1)

            def gates(b, first):
                for n in range(NH):
                    if first and n in TAIL:
                        one(step, TAIL[n])
                    act.wait_ge(g_psum, b * NH + (n + 1))
                    act.activation(sg[:, n % 2, :], pA[n % 2][:], ACT.Silu).then_inc(sg_done, 1)

            gates(0, True)
            with act.Fori(1, NG) as b:
                gates(b, False)

        @block.vector
        def _(dve):
            def rsqrt_op(n, var, sem_inc):
                a, y, h = nw[:, 0, :], nw[:, 1, :], nw[:, 2, :]
                if n == 0:
                    op = dve.tensor_scalar(a, var, EPS, None, ALU.add)
                elif n == 1:
                    op = dve.tensor_scalar(y.bitcast(I32), a.bitcast(I32), -0.5, float(RSQRT_SEED),
                                           ALU.mult, ALU.add)
                elif n % 3 == 2:
                    op = dve.scalar_tensor_tensor(h, y, -0.5, y, ALU.mult, ALU.mult)
                elif n % 3 == 0:
                    op = dve.tensor_tensor(h, h, a, ALU.mult)
                else:
                    op = dve.scalar_tensor_tensor(y, h, 1.5, y, ALU.add, ALU.mult)
                op.then_inc(sem_inc, 1)

            def normalise(dst, t, i, sem_inc):
                dve.tensor_scalar(dst, tile(t), mv[:, i, 0:1], nw[:, 1, i:i + 1], ALU.subtract,
                                  ALU.mult).then_inc(sem_inc, 1)

            def tile(t):
                return z[:, bass.ds(t, 1), :].rearrange("p o d -> p (o d)")

            def ln_op(g, n):
                if n == 0:
                    wait(dve, mv_done, g * 4 + 4)
                wait(dve, ln_ops, g * LN_OPS + n)
                if n < 11:
                    rsqrt_op(n, mv[:, :, 1], ln_ops)
                else:
                    if n == 11:
                        wait(dve, x1_kept, g)
                        wait(dve, x1T_psum, g)
                    normalise(x1s[:, n - 11, :], g * 4 + (n - 11), n - 11, ln_ops)

            def each(v):
                return v.rearrange("p (t o) -> p t o", o=1).broadcast_to([P, 4, E])

            def rt_op(g, n):
                lg = pM[:, 0:4 * E].rearrange("p (t e) -> p t e", e=E)
                ls, ex, pr, eq, key, one1, one2, p2 = (rt_v(i) for i in range(8))
                mx, sm, ri, m1, km, m2, dm, e2, den, w1, w2 = (rs[:, i, :] for i in range(11))
                rev = cst[:, C_REV:C_REV + E].rearrange("p (o e) -> p o e", o=1).broadcast_to([P, 4, E])
                if n == 0:
                    wait(dve, lg_psum, g + 1)
                if n == 2:
                    wait(dve, rt_exp, g * 2 + 1)
                if n == 17:
                    wait(dve, rt_exp, g * 2 + 2)
                wait(dve, rt_ops, g * RT_OPS + n)

                def largest(dst, src):
                    return dve.tensor_reduce(dst, src, AX.X, ALU.max)

                if n == 0:
                    op = largest(mx, lg)
                elif n == 1:
                    op = dve.tensor_tensor(ls, lg, each(mx), ALU.subtract)
                elif n == 2:
                    op = dve.tensor_reduce(sm, ex, AX.X, ALU.add)
                elif n == 3:
                    op = dve.reciprocal(ri, sm)
                elif n == 4:
                    op = dve.tensor_tensor(pr, ex, each(ri), ALU.mult)
                elif n == 5:
                    op = largest(m1, pr)
                elif n == 6:
                    op = dve.tensor_tensor(eq, pr, each(m1), ALU.is_equal)
                elif n == 7:
                    op = dve.tensor_tensor(key, eq, rev, ALU.mult)
                elif n == 8:
                    op = largest(km, key)
                elif n == 9:
                    op = dve.tensor_tensor(one1, key, each(km), ALU.is_equal)
                elif n == 10:
                    op = dve.scalar_tensor_tensor(p2, one1, -2.0, pr, ALU.mult, ALU.add)
                elif n == 11:
                    op = largest(m2, p2)
                elif n == 12:
                    op = dve.tensor_tensor(eq, p2, each(m2), ALU.is_equal)
                elif n == 13:
                    op = dve.tensor_tensor(key, eq, rev, ALU.mult)
                elif n == 14:
                    op = largest(km, key)
                elif n == 15:
                    op = dve.tensor_tensor(one2, key, each(km), ALU.is_equal)
                elif n == 16:
                    op = dve.tensor_tensor(dm, m2, m1, ALU.subtract)
                elif n == 17:
                    op = dve.tensor_scalar(den, e2, 1.0, None, ALU.add)
                elif n == 18:
                    op = dve.reciprocal(w1, den)
                elif n == 19:
                    op = dve.tensor_tensor(w2, e2, w1, ALU.mult)
                elif n == 20:
                    op = dve.tensor_tensor(one1, one1, each(w1), ALU.mult)
                elif n == 21:
                    op = dve.tensor_tensor(one2, one2, each(w2), ALU.mult)
                else:
                    op = dve.tensor_tensor(wt[:, bass.ds(g * 4, 4), :], one1, one2, ALU.add)
                op.then_inc(rt_ops, 1)

            LN_AT = ((0, 1), (2, 3), (4, 5), (6, 7), (8,), (9,), (10,), (11,), (12,))
            RT_AT = ((2,), (3,), (4,), (5,), (6,), (7, 8), (9,), (10, 11), (12,))
            RU_AT = ((13,), (14,), (15,), (16,), (), (17,), (18, 19), (20, 21), (22,))

            dve.wait_ge(s_zero, 3)
            dve.wait_ge(s_kxr, 16)
            dve.tensor_copy(kx[96:P].rearrange("p s c v k -> p (s c v k)"),
                            probs[96:P, 1, 0:4, :].rearrange("p a b -> p (a b)")).then_inc(s_const, 1)

            def step(s, j, ln, tr, rt, ru):
                k, a, w = s + 2, s + 1, s - 2
                if isinstance(s, int) and s == 2:
                    dve.wait_ge(s_z, 16)
                if has(k):
                    wait(dve, k_hi, k + 1)
                    dve.tensor_tensor(kt[64:96, :], pW[64:96, 0:P], kt[64:96, :].bitcast(F32),
                                      ALU.subtract).then_inc(k_lo, 1)
                    wait(dve, v_out, 16 * (k - 1))
                    dve.tensor_copy(vn[:, j % 2, :], pW[:, P:P + KV * HD]).then_inc(v_copied, 1)
                for u in range(NU):
                    if has(s - 3) and u == 0:
                        wait(dve, st_done, s - 2)
                    if has(a):
                        pa = pA[(j + 1 + u) % 2]
                        wait(dve, a_psum, NU * a + u + 1)
                        if u == 0:
                            wait(dve, nm_done, a)
                        if A_UNITS[u] is None:
                            dve.tensor_reduce(mp[:, 2], pa[:].rearrange("p (c v k) -> p c v k", c=CH, v=KV),
                                              AX.X, ALU.max).then_inc(a_max, 1)
                        else:
                            qc, half = A_UNITS[u]
                            dve.tensor_reduce(mp[:, half, qc], pa[:].rearrange("p (i v k) -> p v i k", v=KV, k=C),
                                              AX.XY, ALU.max).then_inc(a_max, 1)
                    if has(s - 3) and u == 0:
                        dve.bn_aggr(mv[:, (j - 3) % 4, :], st6[:, (j - 3) % 4, :]).then_inc(mv_done, 1)
                    if ln is not None:
                        for n in LN_AT[u]:
                            ln_op(ln, n)
                    if tr is not None and u < 2:
                        ln_op(tr, LN_OPS - 2 + u)
                    if rt is not None:
                        for n in RT_AT[u]:
                            rt_op(rt, n)
                    if ru is not None:
                        for n in RU_AT[u]:
                            rt_op(ru, n)
                    if tr is not None and u == 5:
                        wait(dve, x1h_done, tr + 1)
                        dve.tensor_tensor(x1l[:, bass.ds(tr * TC, TC)], x1T[:],
                                          x1h[:, bass.ds(tr * TC, TC)].bitcast(F32), ALU.subtract).then_inc(x1l_done, 1)
                    if tr is not None and u == 8:
                        rt_op(tr, 0)
                        rt_op(tr, 1)
                    if has(k) and u == 1:
                        wait(dve, q_hi, k + 1)
                        ql = q[32:64, (j + 2) % 4, :].rearrange("p (t g) -> p g t", g=G)
                        dve.scalar_tensor_tensor(ql, pQ[32:64, :].rearrange("p (g t) -> p g t", g=G), SCALE,
                                                 ql.bitcast(F32), ALU.mult, ALU.subtract).then_inc(q_lo, 1)
                    if has(w) and u == 2:
                        wait(dve, o_psum, w + 1)
                        wait(dve, den_done, w + 1)
                        wait(dve, attT_psum, w)
                        dve.tensor_tensor(
                            att[:].rearrange("p h g v d -> p g h v d"),
                            pM[0:P // 2, O_AT:DEN_AT].rearrange("p (g h v d) -> p g h v d", g=G, h=2, v=KV),
                            rden[:].rearrange("p g h (v o) -> p g h v o", o=1).broadcast_to([P // 2, G, 2, KV, HD]),
                            ALU.mult).then_inc(att_done, 1)
                    if has(s - 1) and u == 5:
                        wait(dve, den_psum, s)
                        wait(dve, att_done, s - 1)
                        dve.reciprocal(rden[:].rearrange("p g h v -> p (g h v)"),
                                       pM[0:P // 2, DEN_AT:DEN_AT + 2 * G * KV]).then_inc(den_done, 1)
                    if has(w) and u == 7:
                        wait(dve, y_psum, w + 1)
                        dve.tensor_tensor(tile(w), pW[:, 384:512], tile(w), ALU.add).then_inc(z_done, 1)
                if has(w):
                    wait(dve, z_done, w + 1)
                if has(a):
                    wait(dve, a_max, NU * a + NU)
                    wait(dve, m_psum, a)
                    dve.tensor_reduce(nm[:, :, 0:KV], mp[:].rearrange("p n c v -> p c v n"), AX.X, ALU.max,
                                      negate=True).then_inc(nm_done, 1)
                if has(w):
                    dve.bn_stats(st6[:, (j - 2) % 4, :], tile(w)).then_inc(st_done, 1)

            steps(dve, step)
            dve.wait_ge(pv_done, NT - 1)

            def hidden(b, n):
                dve.wait_ge(sg_done, b * NH + (n + 1))
                dve.wait_ge(u_psum, b * NH + (n + 1))
                wait(dve, d_psum, b * E + ((n - 4) // 2 + 1))
                dve.tensor_tensor(hid[:, n % 4, :], sg[:, n % 2, :], pB[n % 2][:], ALU.mult).then_inc(h_done, 1)

            def accumulate(b, e):
                bank = (pO, pW)[e % 2]
                dve.wait_ge(d_psum, b * E + (e + 1))
                wait(dve, acc_done, b * E + e)
                for t in range(4):
                    op = dve.scalar_tensor_tensor(
                        tile(b * 4 + t), bank[:, t * P:(t + 1) * P],
                        wt[:, bass.ds(b * 4 + t, 1), e], tile(b * 4 + t), ALU.mult, ALU.add)
                op.then_inc(acc_done, 1)

            def ln2_op(b, n):
                if n >= 8:
                    wait(dve, ln2_ops, b * LN2_OPS + n)
                if n < 4:
                    dve.bn_stats(st6[:, n, :], tile(b * 4 + n)).then_inc(ln2_ops, 1)
                elif n < 8:
                    dve.bn_aggr(mv[:, n - 4, :], st6[:, n - 4, :]).then_inc(ln2_ops, 1)
                elif n < 19:
                    rsqrt_op(n - 8, mv[:, :, 1], ln2_ops)
                else:
                    normalise(tile(b * 4 + (n - 19)), b * 4 + (n - 19), n - 19, ln2_ops)

            def experts(b, before):
                for n in range(NH):
                    if before is None and n in TAIL:
                        one(step, TAIL[n])
                    if before is not None and n == 3:
                        dve.wait_ge(acc_done, before * E + E)
                    if before is not None and n == 4:
                        dve.wait_ge(ln2_ops, before * LN2_OPS + 4)
                    hidden(b, n)
                    if n >= 4 and n % 2 == 0:
                        accumulate(b, (n - 4) // 2)
                    if before is not None and n in (0, 2):
                        accumulate(before, E - 2 + n // 2)
                    if before is not None and n >= 3:
                        first, last = ((0, 4), (4, 8))[n - 3] if n < 5 else (2 * n - 2, 2 * n)
                        for i in range(first, min(last, LN2_OPS)):
                            ln2_op(before, i)

            dve.wait_ge(x1_kept, 1)
            experts(0, None)
            dve.wait_ge(x1_kept, NG)
            with dve.Fori(1, NG) as b:
                experts(b, b - 1)
            accumulate(NG - 1, E - 2)
            accumulate(NG - 1, E - 1)
            for n in range(LN2_OPS):
                if n == 0:
                    dve.wait_ge(acc_done, NG * E)
                if n == 4:
                    dve.wait_ge(ln2_ops, (NG - 1) * LN2_OPS + 4)
                ln2_op(NG - 1, n)


def constants():
    cst = np.zeros((P, C_END), np.float32)
    cst[:, C_ID:C_ID + P] = np.eye(P)
    for slot in range(4):
        for t in range(NT):
            j = t % 4
            outside = (t % TPS == 0 and slot == (j - 1) % 4) or (t % TPS == TPS - 1 and slot == (j + 1) % 4)
            cst[100 + slot, C_FLAG + t] = -BIG if outside else 0.0
    cst[:, C_REV:C_REV + E] = np.arange(E, 0, -1)
    cst[:, C_ONES:C_ADD] = np.arange(P)[:, None] // C == np.arange(KV)
    row, col = np.arange(P)[:, None], np.arange(2 * VW)
    cst[:, C_ADD:C_END] = (row // 64 == col // VW) & (row % VW == col % VW)
    m = cst[0:C, C_MASK:C_ONES].reshape(C, 6, P)
    row = np.arange(C)[:, None]
    tok_g = np.arange(P)[None, :] // G
    v_tok = np.arange(P)[None, :] % C
    m[:, ONE_Q] = row == tok_g
    m[:, A_LEFT] = np.where(v_tok < row, -BIG, 0.0)
    m[:, A_RIGHT] = np.where(v_tok > row, -BIG, 0.0)
    m[:, ONE_K] = row == v_tok
    m[:, B_LEFT] = np.where(row < tok_g, -BIG, 0.0)
    m[:, B_RIGHT] = np.where(row > tok_g, -BIG, 0.0)
    kx_rows = np.zeros((C, 4, CH, KV, C), np.float32)
    for v in range(KV):
        kx_rows[v, :, :, v, :] = 1.0
    for slot in range(4):
        kx_rows[4 + slot, slot] = 1.0
    blocks = np.zeros((P, KV), np.float32)
    for r in range(96):
        blocks[r, (r % 32) // HD] = 1.0
    return cst, kx_rows.reshape(C, 4, TC), blocks


def kernel(L0_attn_x, L0_attn_Wq, L0_attn_Wk, L0_attn_Wv, L0_attn_Wo, L0_ffn_kernel_router_DE,
           L0_ffn_kernel_gating_EDF, L0_ffn_kernel_up_EDF, L0_ffn_kernel_down_EFD):
    from concourse import bacc
    from concourse.bass_utils import run_bass_kernel_spmd

    x = np.ascontiguousarray(L0_attn_x).reshape(TOK, D)
    w_q = np.asarray(L0_attn_Wq).reshape(KV, G, HD, D).transpose(3, 1, 0, 2).reshape(D, G, 1, KV * HD)
    wq = np.zeros((D, G, P), np.float32)
    wq[:, :, 0:96] = np.broadcast_to(w_q, (D, G, 3, KV * HD)).reshape(D, G, 96)
    w_k = np.asarray(L0_attn_Wk).T.reshape(D, 1, KV * HD)
    cst, kx_rows, blocks = constants()
    arrays = {
        "x": x,
        "xT": np.ascontiguousarray(x.T),
        "wq": wq,
        "wk": np.ascontiguousarray(np.broadcast_to(w_k, (D, 3, KV * HD)).reshape(D, 96)),
        "wv": np.ascontiguousarray(np.asarray(L0_attn_Wv).T),
        "wo": np.ascontiguousarray(np.asarray(L0_attn_Wo).reshape(D, KV, G, HD).transpose(2, 1, 3, 0).reshape(P, D)),
        "wr": np.ascontiguousarray(L0_ffn_kernel_router_DE),
        "wg": np.ascontiguousarray(np.asarray(L0_ffn_kernel_gating_EDF).transpose(1, 0, 2).reshape(D, E * F)),
        "wu": np.ascontiguousarray(np.asarray(L0_ffn_kernel_up_EDF).transpose(1, 0, 2).reshape(D, E * F)),
        "wd": np.ascontiguousarray(
            np.asarray(L0_ffn_kernel_down_EFD).reshape(E * FH, P, D).transpose(1, 0, 2)),
        "consts": cst,
        "kx_rows": kx_rows,
        "blocks": blocks,
    }
    nc = bacc.Bacc("TRN2", target_bir_lowering=False, num_devices=1)
    ins = [nc.dram_tensor(n, a.shape, mybir.dt.from_np(a.dtype), kind="ExternalInput").ap() for n, a in arrays.items()]
    out = nc.dram_tensor("out", (TOK, D), F32, kind="ExternalOutput").ap()
    v_scr = nc.dram_tensor("v_scr", (NT, P, KV * HD), F32, kind="Internal").ap()
    attention_moe(nc, *ins, out, v_scr)
    r = run_bass_kernel_spmd(nc, [arrays], core_ids=[0])
    return r.results[0]["out"].reshape(NB, SEQ, D)
```
